# Optimizing a Trainium2 kernel written in Bass

```python
import numpy as np
import jax
import jax.numpy as jnp

def _softmax(x, axis=-1):
    return jax.nn.softmax(x, axis=axis)

def _gelu(x):
    return jax.nn.gelu(x, approximate=True)

def _silu(x):
    return jax.nn.silu(x)

def _sigmoid(x):
    return jax.nn.sigmoid(x)

def _layernorm(x, axis=-1, eps=1e-05):
    m = jnp.mean(x, axis=axis, keepdims=True)
    v = jnp.var(x, axis=axis, keepdims=True)
    return (x - m) / jnp.sqrt(v + eps)

def _scatter_add(tgt, idx, src, axis=0):
    return tgt.at[idx].add(src)

def _segment_sum(src, seg, n):
    return jax.ops.segment_sum(src, seg, n)
kernel_name = 'mk_rec_standalone_d1_rec_r8_a8a33e'

def setup_inputs(seed: int=0):
    np.random.seed(seed)
    _w = jnp.asarray

    def _rec_inputs():
        import jax
        import jax.numpy as jnp
        _rk = jax.random.key(seed)
        r_x = -0.000392918 + 0.999932 * jax.random.normal(jax.random.fold_in(_rk, 1), (2048, 1024), jnp.float32)
        return r_x
    r_x = _rec_inputs()

    def _L0_rec_setup():
        import jax, jax.numpy as jnp
        import numpy as np
        BN_EPS = 0.001
        LN_EPS = 1e-06
        key = jax.random.key(seed)
        B, D, U = (2048, 1024, 1024)
        ks = jax.random.split(key, 8)
        s_in, s_hid, s_out = (1.0 / np.sqrt(D), 1.0 / np.sqrt(U), 1.0 / np.sqrt(3 * U))
        return {'x': jax.random.normal(ks[0], (B, D), jnp.float32), 'linear_w': jax.random.normal(ks[1], (D, U), jnp.float32) * s_in, 'linear_b': jnp.zeros((U,), jnp.float32), 'deep1_w': jax.random.normal(ks[2], (D, U), jnp.float32) * s_in, 'deep1_b': jnp.zeros((U,), jnp.float32), 'deep2_w': jax.random.normal(ks[3], (U, U), jnp.float32) * s_hid, 'deep2_b': jnp.zeros((U,), jnp.float32), 'cross_w': jax.random.normal(ks[4], (D, D), jnp.float32) * s_in, 'cross_b': jnp.zeros((D,), jnp.float32), 'proj_w': jax.random.normal(ks[5], (D, U), jnp.float32) * s_in, 'proj_b': jnp.zeros((U,), jnp.float32), 'bn_gamma': jnp.ones((3 * U,), jnp.float32), 'bn_beta': jnp.zeros((3 * U,), jnp.float32), 'bn_mean': jnp.zeros((3 * U,), jnp.float32), 'bn_var': jnp.ones((3 * U,), jnp.float32), 'out_w': jax.random.normal(ks[6], (3 * U, U), jnp.float32) * s_out, 'out_b': jnp.zeros((U,), jnp.float32), 'ln_gamma': jnp.ones((U,), jnp.float32), 'ln_beta': jnp.zeros((U,), jnp.float32)}
    _L0_rec_all = _L0_rec_setup()
    _L0_rec_in = {k: v for k, v in _L0_rec_all.items() if k in ('linear_w', 'linear_b', 'deep1_w', 'deep1_b', 'deep2_w', 'deep2_b', 'cross_w', 'cross_b', 'proj_w', 'proj_b', 'bn_gamma', 'bn_beta', 'bn_mean', 'bn_var', 'out_w', 'out_b', 'ln_gamma', 'ln_beta')}
    del _L0_rec_all
    return {'r_x': r_x, 'L0_rec_linear_w': _L0_rec_in['linear_w'], 'L0_rec_linear_b': _L0_rec_in['linear_b'], 'L0_rec_deep1_w': _L0_rec_in['deep1_w'], 'L0_rec_deep1_b': _L0_rec_in['deep1_b'], 'L0_rec_deep2_w': _L0_rec_in['deep2_w'], 'L0_rec_deep2_b': _L0_rec_in['deep2_b'], 'L0_rec_cross_w': _L0_rec_in['cross_w'], 'L0_rec_cross_b': _L0_rec_in['cross_b'], 'L0_rec_proj_w': _L0_rec_in['proj_w'], 'L0_rec_proj_b': _L0_rec_in['proj_b'], 'L0_rec_bn_gamma': _L0_rec_in['bn_gamma'], 'L0_rec_bn_beta': _L0_rec_in['bn_beta'], 'L0_rec_bn_mean': _L0_rec_in['bn_mean'], 'L0_rec_bn_var': _L0_rec_in['bn_var'], 'L0_rec_out_w': _L0_rec_in['out_w'], 'L0_rec_out_b': _L0_rec_in['out_b'], 'L0_rec_ln_gamma': _L0_rec_in['ln_gamma'], 'L0_rec_ln_beta': _L0_rec_in['ln_beta']}

def reference(r_x, L0_rec_linear_w, L0_rec_linear_b, L0_rec_deep1_w, L0_rec_deep1_b, L0_rec_deep2_w, L0_rec_deep2_b, L0_rec_cross_w, L0_rec_cross_b, L0_rec_proj_w, L0_rec_proj_b, L0_rec_bn_gamma, L0_rec_bn_beta, L0_rec_bn_mean, L0_rec_bn_var, L0_rec_out_w, L0_rec_out_b, L0_rec_ln_gamma, L0_rec_ln_beta):
    import jax
    import jax.numpy as jnp

    def _L0_rec_ref(x, linear_w, linear_b, deep1_w, deep1_b, deep2_w, deep2_b, cross_w, cross_b, proj_w, proj_b, bn_gamma, bn_beta, bn_mean, bn_var, out_w, out_b, ln_gamma, ln_beta):
        import jax, jax.numpy as jnp
        import numpy as np
        BN_EPS = 0.001
        LN_EPS = 1e-06
        linear_out = x @ linear_w + linear_b
        deep_out = jax.nn.silu(x @ deep1_w + deep1_b)
        deep_out = jax.nn.silu(deep_out @ deep2_w + deep2_b)
        cross_term = x * (x @ cross_w.T) + cross_b
        cross_out = cross_term @ proj_w + proj_b
        combined = jnp.concatenate([linear_out, deep_out, cross_out], axis=-1)
        combined = (combined - bn_mean) * jax.lax.rsqrt(bn_var + BN_EPS) * bn_gamma + bn_beta
        out = jax.nn.silu(combined @ out_w + out_b)
        mu = jnp.mean(out, axis=-1, keepdims=True)
        var = jnp.mean(jnp.square(out - mu), axis=-1, keepdims=True)
        out = (out - mu) * jax.lax.rsqrt(var + LN_EPS) * ln_gamma + ln_beta
        return out
    y = _L0_rec_ref(r_x, L0_rec_linear_w, L0_rec_linear_b, L0_rec_deep1_w, L0_rec_deep1_b, L0_rec_deep2_w, L0_rec_deep2_b, L0_rec_cross_w, L0_rec_cross_b, L0_rec_proj_w, L0_rec_proj_b, L0_rec_bn_gamma, L0_rec_bn_beta, L0_rec_bn_mean, L0_rec_bn_var, L0_rec_out_w, L0_rec_out_b, L0_rec_ln_gamma, L0_rec_ln_beta)
    return y

_drawn_inputs = setup_inputs


def setup_inputs(seed=0):
    import zlib

    import numpy as np

    out = dict(_drawn_inputs(seed))
    spreads = {'L0_rec_linear_b': (0.0, 0.1),
     'L0_rec_deep1_b': (0.0, 0.325),
     'L0_rec_deep2_b': (0.0, 0.1),
     'L0_rec_cross_b': (0.0, 0.1),
     'L0_rec_proj_b': (0.0, 0.1),
     'L0_rec_bn_gamma': (1.0, 0.2),
     'L0_rec_bn_beta': (0.0, 0.1),
     'L0_rec_bn_mean': (0.0, 0.1),
     'L0_rec_bn_var': (1.0, 0.2),
     'L0_rec_out_b': (0.0, 0.1),
     'L0_rec_ln_gamma': (1.0, 0.2),
     'L0_rec_ln_beta': (0.0, 0.1)}
    factors = {}
    for name, (base, spread) in spreads.items():
        noise = np.random.default_rng([zlib.crc32(name.encode()), seed]).standard_normal(out[name].shape)
        drawn = base * np.exp(spread * noise) if base else spread * noise
        out[name] = jnp.asarray(drawn.astype(out[name].dtype))
    for name, factor in factors.items():
        out[name] = (out[name] * factor).astype(out[name].dtype)
    return out
```

```python
from contextlib import ExitStack

import concourse.bass as bass
from concourse import mybir

P = 128
ROWS, D = 2048, 1024
K = D // P
R = 512
BLOCKS = ROWS // R
RT = R // P
N = 512
H = D // N
RING = 4
SPLIT = 2
TILES = 3 * K
HALF = 3 * K // 2
STEPS = TILES + H * HALF
FOLD = 2 * K
OUT_TILES = 3 * K
BN_EPS, LN_EPS = 1e-3, 1e-6

F32 = mybir.dt.float32
F32R = mybir.dt.float32r
ALU = mybir.AluOpType
ACT = mybir.ActivationFunctionType

GAMMA, BETA, MEAN, VAR = (i * 3 * K for i in range(4))
LIN_B, DEEP1_B, DEEP2_B, CROSS_B, PROJ_B = (12 * K + i * K for i in range(5))
PARAMS = 17 * K

OUT_ORDER = list(range(K)) + [t for k in range(K) for t in (2 * K + k, K + k)]


def rec_tower(nc, x_blocks, stream, out_rows, out_deep, params, rows, out):
    ctx = ExitStack()
    with ctx:
        def sb(name, shape, dt=F32):
            return ctx.enter_context(nc.sbuf_tensor(name, shape, dt))

        def sem(name):
            return ctx.enter_context(nc.semaphore(name))

        folded = nc.dram_tensor("folded", [2, H, K // 2, P, 2, N], F32, kind="Internal").ap()

        XH = sb("XH", [P, 4, K, R], F32R)
        CH = sb("CH", [P, 4, K, R], F32R)
        x_raw = sb("x_raw", [P, K, R])
        w_raw = sb("w_raw", [P, RING, D])
        w_split = sb("w_split", [P, SPLIT, 2, D], F32R)
        y = sb("y", [P, RT, D])
        bias_row = sb("bias_row", [P, D])
        ln_gamma = sb("ln_gamma", [P, D])
        ln_beta = sb("ln_beta", [P, D])
        prm = sb("prm", [P, PARAMS])
        scale = sb("scale", [P, 3 * K])
        shift = sb("shift", [P, 3 * K])
        exps = sb("exps", [P, 3 * K])
        ln_eps = sb("ln_eps", [P, 1])
        ones = sb("ones", [P, P])
        stats = sb("stats", [P, RT, H, 6])
        mv = sb("mv", [P, RT, 2])
        rstd = sb("rstd", [P, RT])
        bank = ctx.enter_context(nc.psum_tensor("bank", [P, 8, N], F32))
        bias_part, fold_out = ln_gamma, ln_beta

        prm_loaded = sem("prm_loaded")
        x_loaded = sem("x_loaded")
        ln_loaded = sem("ln_loaded")
        w_loaded = [sem(f"w_loaded{i}") for i in range(RING)]
        y_moved = [sem(f"y_moved{i}") for i in range(RING)]
        outb_loaded = sem("outb_loaded")
        pool_const = sem("pool_const")
        rstd_bn = sem("rstd_bn")
        var_eps = sem("var_eps")
        vec_chain = sem("vec_chain")
        pool_chain = sem("pool_chain")
        w_scaled = sem("w_scaled")
        w_hi = sem("w_hi")
        w_ready = sem("w_ready")
        out_hi = sem("out_hi")
        out_used = sem("out_used")
        rhs_ready = sem("rhs_ready")
        x_hi = sem("x_hi")
        x_ready = sem("x_ready")
        chunk_done = sem("chunk_done")
        bank_free = sem("bank_free")
        bias_done = sem("bias_done")
        fold_stored = [sem(f"fold_stored{n}") for n in range(H)]
        silu_done = sem("silu_done")
        tile_done = sem("tile_done")
        z_biased = sem("z_biased")
        y_ready = sem("y_ready")
        mv_ready = sem("mv_ready")
        rstd_ready = sem("rstd_ready")
        y_normal = sem("y_normal")
        y_final = sem("y_final")

        LAST = BLOCKS - 1
        SEAM = 5
        POOL_CONSTS = 2
        BANKS_FOLD = H * FOLD + H
        Y_FOLD = 16 * (OUT_TILES // RING)

        block = ctx.enter_context(nc.Block())

        @block.sync
        def _(sp):
            def load_chunk(c, slot, src):
                if not isinstance(c, int) or c >= RING:
                    sp.wait_ge(w_ready, c - RING + 1)
                sp.dma_start(w_raw[:, slot, :], src).then_inc(w_loaded[slot], 16)

            def load_out_tile(i):
                if i >= RING:
                    sp.wait_ge(out_used, i - RING + 1)
                sp.dma_start(y[:, i % RING, :], out_rows[OUT_ORDER[i]]).then_inc(y_moved[i % RING], 16)

            def fold_chunk(c):
                if c < FOLD:
                    load_chunk(c, c % RING, stream[c])

            sp.dma_start(prm[:, :], params).then_inc(prm_loaded, 16)
            fold_chunk(0)
            for i in range(RING):
                load_out_tile(i)
            fold_chunk(1)
            for i in range(RING, K):
                load_out_tile(i)
                if i % 2:
                    fold_chunk(i // 2)
            sp.dma_start(x_raw[:, :, :], x_blocks[0]).then_inc(x_loaded, 16)
            for j in range(K):
                load_out_tile(K + 2 * j)
                load_out_tile(K + 2 * j + 1)
                fold_chunk(RING + j)
            for c in range(RING + K, FOLD):
                fold_chunk(c)

            def first(b):
                return FOLD + STEPS * b

            def tile_loads(b):
                with sp.Fori(0, TILES // RING) as t:
                    for u in range(RING):
                        i = t * RING + u
                        load_chunk(first(b) + i, u, stream[bass.ds(i + FOLD, 1)].rearrange("a p n -> (a p) n"))

            def x_load(b):
                sp.wait_ge(tile_done, TILES * (b - 1) + 2 * K)
                sp.wait_ge(x_ready, K * b)
                sp.dma_start(x_raw[:, :, :],
                             x_blocks[bass.ds(b, 1)].rearrange("a p k r -> (a p) k r")).then_inc(x_loaded, 16)

            def z_loads(b):
                for n in range(H):
                    for q in range(HALF):
                        src = out_deep[n, q - K] if q >= K else folded[q // (K // 2), n, q % (K // 2)].rearrange(
                            "p a n -> p (a n)")
                        load_chunk(first(b) + TILES + HALF * n + q, q % RING, src)

            def stores(b):
                for r in range(RT):
                    sp.wait_ge(y_final, RT * b + (r + 1))
                    sp.dma_start(out[bass.ds((RT * b + r) * P, P), :], y[:, r, :]).then_inc(y_moved[r], 16)

            tile_loads(0)
            for n in range(H):
                sp.wait_ge(fold_stored[n], 16 * FOLD)
            with sp.Fori(0, LAST) as b:
                x_load(b + 1)
                z_loads(b)
                tile_loads(b + 1)
                stores(b)
            z_loads(LAST)
            stores(LAST)
            for r in range(RT):
                sp.wait_ge(y_moved[r], Y_FOLD + 16 * BLOCKS)

        @block.tensor
        def _(pe):
            def three(out_ap, hi_l, lo_l, hi_r, lo_r, start, stop):
                nc.tensor.matmul(out_ap, hi_l, hi_r, start=start, stop=False)
                nc.tensor.matmul(out_ap, hi_l, lo_r, start=False, stop=False)
                return nc.tensor.matmul(out_ap, lo_l, hi_r, start=False, stop=stop)

            def half_of_chunk(c, h):
                return w_split[:, c % SPLIT, h, :].rearrange("p (k m) -> p k m", k=K)

            def fold_chunks(f, rhs, base):
                for u in range(4):
                    c = base + u
                    hi, lo = half_of_chunk(u, 0), half_of_chunk(u, 1)
                    pe.wait_ge(w_ready, c + 1)
                    for k in range(K):
                        pe.wait_ge(rhs_ready, f * K + k + 1)
                        for n in range(H):
                            if k == 0 and not (isinstance(c, int) and c < 4):
                                pe.wait_ge(bank_free, H * (c - 4) + n + 1)
                            last = three(bank[:, H * u + n, :], hi[:, k, :], lo[:, k, :],
                                         rhs[:, n, k, :], rhs[:, 2 + n, k, :], k == 0, k == K - 1)
                    last.then_inc(chunk_done, 1)

            fold_chunks(0, XH, 0)
            fold_chunks(0, XH, 4)
            with pe.Fori(0, K // 4) as t:
                fold_chunks(1, CH, t * 4 + K)
            pe.wait_ge(bank_free, H * FOLD - 2)
            pe.wait_ge(out_used, OUT_TILES)
            pe.wait_ge(pool_const, 1)
            for n in range(H):
                last = nc.tensor.matmul(bank[:, 4 + n, :], ones[:, :], bias_part[:, n * N:(n + 1) * N],
                                        start=True, stop=True)
            last.then_inc(bias_done, 1)

            def feature_tiles(b, at, src):
                for m in range(K):
                    c = FOLD + STEPS * b + at + m
                    hi, lo = half_of_chunk(m, 0), half_of_chunk(m, 1)
                    pe.wait_ge(w_ready, c + 1)
                    if at == 0 and m == 0:
                        pe.wait_ge(bank_free, 2 * RT * b + BANKS_FOLD - RT)
                    elif at == 0 and m == RT:
                        pe.wait_ge(bank_free, 2 * RT * b + BANKS_FOLD)
                    elif at:
                        pe.wait_ge(tile_done, TILES * b + (at + m - K + 1))
                    for k in range(K):
                        if at == 0 and m == 0:
                            pe.wait_ge(x_ready, K * b + k + 1)
                        last = three(bank[:, m, :], hi[:, k, :], lo[:, k, :],
                                     XH[:, src, k, :], XH[:, src + 1, k, :], k == 0, k == K - 1)
                    last.then_inc(chunk_done, 1)

            def z_half(b, n):
                for q in range(HALF):
                    c = FOLD + STEPS * b + TILES + HALF * n + q
                    pe.wait_ge(w_ready, c + 1)
                    if q == 0:
                        pe.wait_ge(tile_done, TILES * b + (TILES - K + RT) + RT * n)
                    if q == K:
                        pe.wait_ge(tile_done, TILES * b + TILES)
                    act, at = ((XH, 0), (CH, 0), (CH, 2))[q // (K // 2)]
                    for a in range(2):
                        k = 2 * (q % (K // 2)) + a
                        w_hi_k = w_split[:, q % SPLIT, 0, a * N:(a + 1) * N]
                        w_lo_k = w_split[:, q % SPLIT, 1, a * N:(a + 1) * N]
                        for r in range(RT):
                            last = three(bank[:, bass.ds(RT * n + r, 1), :].rearrange("p a n -> p (a n)"),
                                         act[:, at, k, r * P:(r + 1) * P],
                                         act[:, at + 1, k, r * P:(r + 1) * P], w_hi_k, w_lo_k,
                                         q == 0 and a == 0, q == HALF - 1 and a == 1)
                    last.then_inc(chunk_done, 1)

            with pe.Fori(0, BLOCKS) as b:
                feature_tiles(b, 0, 0)
                feature_tiles(b, K, 0)
                feature_tiles(b, 2 * K, 2)
                with pe.Fori(0, H) as n:
                    z_half(b, n)

        @block.scalar
        def _(act):
            def split_hi(c, slot):
                if isinstance(c, int) and c < FOLD:
                    act.wait_ge(w_scaled, c + 1)
                else:
                    act.wait_ge(w_loaded[slot], 4 * (c - slot) + 16)
                if not isinstance(c, int) or c >= SPLIT:
                    act.wait_ge(chunk_done, c - SPLIT + 1)
                nc.scalar.activation(w_split[:, slot % SPLIT, 0, :], w_raw[:, slot, :], ACT.Copy).then_inc(w_hi, 1)

            def out_tile_hi(i):
                if i >= K and (i - K) % 2:
                    return
                act.wait_ge(y_moved[i % RING], 16 * (i // RING + 1))
                dst, k = (XH, i) if i < K else (CH, (i - K) // 2)
                nc.scalar.activation(dst[:, 0:H, k, :], y[:, i % RING, :].rearrange("p (h n) -> p h n", h=H),
                                     ACT.Copy).then_inc(out_hi, 1)

            def x_split_hi(b, k):
                act.wait_ge(x_loaded, 16 * b + 16)
                nc.scalar.activation(XH[:, 0, k, :], x_raw[:, k, :], ACT.Copy).then_inc(x_hi, 1)

            def silu_tile(c, bank_at, bias_at, done):
                act.wait_ge(chunk_done, c + 1)
                nc.scalar.activation(bank_at, bank_at, ACT.Silu, bias=bias_at).then_inc(done, 1)

            split_hi(0, 0)
            for i in range(K):
                out_tile_hi(i)
            split_hi(1, 1)
            for j in range(FOLD):
                split_hi(j + SPLIT, (j + SPLIT) % RING)
                for n in range(H):
                    if j:
                        act.wait_ge(fold_stored[n], 16 * j)
                    nc.scalar.activation(fold_out[:, n * N:(n + 1) * N], bank[:, H * (j % 4) + n, :],
                                         ACT.Copy).then_inc(bank_free, 1)
                if j < K:
                    out_tile_hi(K + 2 * j)
                if K - 1 <= j < 2 * K - 1:
                    x_split_hi(0, j - (K - 1))
            act.wait_ge(bias_done, 1)
            for n in range(H):
                nc.scalar.activation(bias_row[:, n * N:(n + 1) * N], bank[:, 4 + n, :], ACT.Copy).then_inc(bank_free, 1)

            def silu_z(b, n, r):
                act.wait_ge(y_moved[r], 16 * b + Y_FOLD)
                act.wait_ge(z_biased, 2 * RT * b + RT * n + r + 1)
                nc.scalar.activation(y[:, r, n * N:(n + 1) * N], bank[:, RT * n + r, :],
                                     ACT.Silu).then_inc(bank_free, 1)

            def first(b):
                return FOLD + STEPS * b

            def h_tile(b, j, m, slot, bias_at):
                c = first(b) + j
                split_hi(c + SPLIT, (slot + SPLIT) % RING)
                silu_tile(c, bank[:, bass.ds(m, 1), :].rearrange("p a n -> p (a n)"),
                          prm[:, bass.ds(bias_at + m, 1)], silu_done)

            def seam(b, z):
                for j in range(SEAM):
                    h_tile(b, j, j, j % RING, DEEP1_B)
                    if z and j < 2:
                        for r in (2 * j, 2 * j + 1):
                            silu_z(b - 1, 1, r)

            def body(b, last):
                for j in range(SEAM, K):
                    h_tile(b, j, j, j % RING, DEEP1_B)
                with act.Fori(0, K // RING) as t:
                    for u in range(RING):
                        split_hi(first(b) + t * RING + (K + u + SPLIT), (u + SPLIT) % RING)
                with act.Fori(0, K // RING) as t:
                    for u in range(RING):
                        m = t * RING + u
                        h_tile(b, m + 2 * K, m, u, DEEP2_B)
                with act.Fori(0, HALF // RING) as t:
                    for u in range(RING):
                        split_hi(first(b) + t * RING + (TILES + u + SPLIT), (u + SPLIT) % RING)
                for q in range(HALF):
                    j = TILES + HALF + q
                    if not (last and q >= HALF - SPLIT):
                        split_hi(first(b) + j + SPLIT, (j + SPLIT) % RING)
                    if q < 2:
                        for r in (2 * q, 2 * q + 1):
                            silu_z(b, 0, r)
                    if not last and K // 2 - 1 <= q < K // 2 - 1 + K:
                        x_split_hi(b + 1, q - (K // 2 - 1))

            seam(0, False)
            with act.Fori(0, LAST) as b:
                body(b, False)
                seam(b + 1, True)
            body(LAST, True)
            for r in range(RT):
                silu_z(LAST, 1, r)

        @block.vector
        def _(dve):
            chain = [0]

            def link(ins):
                chain[0] += 1
                ins.then_inc(vec_chain, 1)
                dve.wait_ge(vec_chain, chain[0])

            dve.wait_ge(prm_loaded, 16)
            nc.vector.tensor_scalar(scale[:, :], prm[:, VAR:VAR + 3 * K], BN_EPS, None, ALU.add).then_inc(var_eps, 1)
            nc.vector.memset(bias_part[:, :], 0.0).then_inc(var_eps, 1)
            dve.wait_ge(rstd_bn, 1)
            link(nc.vector.tensor_tensor(scale[:, :], scale[:, :], prm[:, GAMMA:GAMMA + 3 * K], ALU.mult))
            link(nc.vector.tensor_scalar(shift[:, :], prm[:, MEAN:MEAN + 3 * K], -1.0, None, ALU.mult))
            link(nc.vector.tensor_tensor(shift[:, 0:K], shift[:, 0:K], prm[:, LIN_B:LIN_B + K], ALU.add))
            link(nc.vector.tensor_tensor(shift[:, 2 * K:3 * K], shift[:, 2 * K:3 * K],
                                         prm[:, PROJ_B:PROJ_B + K], ALU.add))
            link(nc.vector.tensor_tensor(shift[:, :], shift[:, :], scale[:, :], ALU.mult))
            link(nc.vector.tensor_tensor(shift[:, :], shift[:, :], prm[:, BETA:BETA + 3 * K], ALU.add))

            def scale_chunk(c):
                if c >= FOLD:
                    return
                branch = 0 if c < K else 2 * K
                dve.wait_ge(w_loaded[c % RING], 16 * (c // RING + 1))
                ap = w_raw[:, c % RING, :].rearrange("p (k m) -> p k m", k=K)
                nc.vector.tensor_tensor(ap, ap, scale[:, branch:branch + K].unsqueeze(2).to_broadcast([P, K, P]),
                                        ALU.mult).then_inc(w_scaled, 1)

            def split_lo(c, slot):
                dve.wait_ge(w_hi, c + 1)
                nc.vector.tensor_tensor(w_split[:, slot % SPLIT, 1, :], w_raw[:, slot, :],
                                        w_split[:, slot % SPLIT, 0, :].bitcast(F32),
                                        ALU.subtract).then_inc(w_ready, 1)

            def out_tile(i):
                src = y[:, i % RING, :]
                if i < K or (i - K) % 2 == 0:
                    dst, k = (XH, i) if i < K else (CH, (i - K) // 2)
                    dve.wait_ge(out_hi, (i if i < K else K + (i - K) // 2) + 1)
                    nc.vector.tensor_tensor(dst[:, 2:4, k, :], src.rearrange("p (h n) -> p h n", h=H),
                                            dst[:, 0:2, k, :].bitcast(F32), ALU.subtract).then_inc(rhs_ready, 1)
                else:
                    dve.wait_ge(y_moved[i % RING], 16 * (i // RING + 1))
                t = OUT_ORDER[i]
                if i == 0:
                    dve.wait_ge(outb_loaded, 16)
                else:
                    dve.wait_ge(out_used, i)
                nc.vector.scalar_tensor_tensor(out=bias_part[:, :], in0=src, scalar=shift[:, t:t + 1],
                                               in1=bias_part[:, :], op0=ALU.mult, op1=ALU.add).then_inc(out_used, 1)

            def x_split_lo(b, k):
                dve.wait_ge(x_hi, K * b + k + 1)
                nc.vector.tensor_tensor(XH[:, 1, k, :], x_raw[:, k, :], XH[:, 0, k, :].bitcast(F32),
                                        ALU.subtract).then_inc(x_ready, 1)

            scale_chunk(0)
            split_lo(0, 0)
            for i in range(K):
                out_tile(i)
            scale_chunk(1)
            split_lo(1, 1)
            for j in range(FOLD):
                scale_chunk(j + SPLIT)
                split_lo(j + SPLIT, (j + SPLIT) % RING)
                if j < K:
                    out_tile(K + 2 * j)
                    out_tile(K + 2 * j + 1)
                if K - 1 <= j < 2 * K - 1:
                    x_split_lo(0, j - (K - 1))
            dve.wait_ge(bank_free, BANKS_FOLD)

            def first(b):
                return FOLD + STEPS * b

            def at(tensor, m):
                return tensor[:, bass.ds(m, 1), :].rearrange("p a n -> p (a n)")

            def h1_tile(b, j, slot):
                split_lo(first(b) + j + SPLIT, (slot + SPLIT) % RING)
                dve.wait_ge(silu_done, 2 * K * b + (j + 1))
                nc.vector.tensor_copy(XH[:, 2, j, :], bank[:, j, :]).then_inc(vec_chain, 1)
                dve.wait_ge(vec_chain, chain_at(b, H1_LINK + j))
                nc.vector.tensor_tensor(XH[:, 3, j, :], bank[:, j, :], XH[:, 2, j, :].bitcast(F32),
                                        ALU.subtract).then_inc(tile_done, 1)

            H1_LINK, C_LINK, H2_LINK, LINKS = 1, K + 1, 3 * K + 1, 4 * K
            chain_before = chain[0]

            def chain_at(b, i):
                return LINKS * b + (chain_before + i)

            def c_tile(b, m, slot):
                split_lo(first(b) + K + m + SPLIT, (slot + SPLIT) % RING)
                dve.wait_ge(chunk_done, first(b) + K + m + 1)
                acc = at(bank, m)
                bias = prm[:, bass.ds(CROSS_B + m, 1)]
                nc.vector.tensor_tensor(acc, acc, at(x_raw, m), ALU.mult).then_inc(vec_chain, 1)
                dve.wait_ge(vec_chain, chain_at(b, 2 * m + C_LINK))
                nc.vector.tensor_scalar(at(CH[:, 0], m), acc, bias, None, ALU.add).then_inc(vec_chain, 1)
                dve.wait_ge(vec_chain, chain_at(b, 2 * m + C_LINK + 1))
                nc.vector.scalar_tensor_tensor(out=at(CH[:, 1], m), in0=acc, scalar=bias,
                                               in1=at(CH[:, 0], m).bitcast(F32), op0=ALU.add,
                                               op1=ALU.subtract).then_inc(tile_done, 1)

            def h2_tile(b, m, slot):
                split_lo(first(b) + 2 * K + m + SPLIT, (slot + SPLIT) % RING)
                dve.wait_ge(silu_done, 2 * K * b + K + m + 1)
                acc = at(bank, m)
                s = scale[:, bass.ds(K + m, 1)]
                nc.vector.tensor_scalar(at(CH[:, 2], m), acc, s, None, ALU.mult).then_inc(vec_chain, 1)
                dve.wait_ge(vec_chain, chain_at(b, m + H2_LINK))
                nc.vector.scalar_tensor_tensor(out=at(CH[:, 3], m), in0=acc, scalar=s,
                                               in1=at(CH[:, 2], m).bitcast(F32), op0=ALU.mult,
                                               op1=ALU.subtract).then_inc(tile_done, 1)

            def add_bias(b, n, r):
                dve.wait_ge(chunk_done, first(b) + TILES + HALF * (n + 1))
                nc.vector.tensor_tensor(bank[:, RT * n + r, :], bank[:, RT * n + r, :],
                                        bias_row[:, n * N:(n + 1) * N], ALU.add).then_inc(z_biased, 1)

            def row_stats(b, n, r):
                dve.wait_ge(bank_free, 2 * RT * b + (BANKS_FOLD + RT * n + r + 1))
                nc.vector.bn_stats(stats[:, r, n, :], y[:, r, n * N:(n + 1) * N]).then_inc(y_ready, 1)

            def stats_written(b, r):
                dve.wait_ge(y_ready, 2 * RT * b + (RT + r + 1))

            def row_aggregate(b, r):
                nc.vector.bn_aggr(mv[:, r, :], stats[:, r, :, :].rearrange("p h s -> p (h s)")).then_inc(mv_ready, 1)

            def row_normalise(b, r):
                dve.wait_ge(rstd_ready, RT * b + (r + 1))
                nc.vector.tensor_scalar(y[:, r, :], y[:, r, :], mv[:, r, 0:1], rstd[:, r:r + 1],
                                        ALU.subtract, ALU.mult).then_inc(y_normal, 1)

            def seam(b, z):
                for j in range(SEAM):
                    if z and 2 <= j < 4:
                        stats_written(b - 1, 2 * j - 3)
                    h1_tile(b, j, j % RING)
                    if z and j < 2:
                        for r in (2 * j, 2 * j + 1):
                            add_bias(b - 1, 1, r)
                    if z and 1 <= j < 3:
                        for r in (2 * j - 2, 2 * j - 1):
                            row_stats(b - 1, 1, r)
                    if z and 2 <= j < 4:
                        for r in (2 * j - 4, 2 * j - 3):
                            row_aggregate(b - 1, r)
                    if z and 3 <= j < 5:
                        for r in (2 * j - 6, 2 * j - 5):
                            row_normalise(b - 1, r)

            def body(b, last):
                for j in range(SEAM, K):
                    h1_tile(b, j, j % RING)
                with dve.Fori(0, K // RING) as t:
                    for u in range(RING):
                        c_tile(b, t * RING + u, u)
                with dve.Fori(0, K // RING) as t:
                    for u in range(RING):
                        h2_tile(b, t * RING + u, u)
                with dve.Fori(0, HALF // RING) as t:
                    for u in range(RING):
                        split_lo(first(b) + t * RING + (TILES + u + SPLIT), (u + SPLIT) % RING)
                for q in range(HALF):
                    if not (last and q >= HALF - SPLIT):
                        split_lo(first(b) + TILES + HALF + q + SPLIT, (q + SPLIT) % RING)
                    if q < 2:
                        for r in (2 * q, 2 * q + 1):
                            add_bias(b, 0, r)
                    if 1 <= q < 3:
                        for r in (2 * q - 2, 2 * q - 1):
                            row_stats(b, 0, r)
                    if not last and K // 2 - 1 <= q < K // 2 - 1 + K:
                        x_split_lo(b + 1, q - (K // 2 - 1))

            seam(0, False)
            with dve.Fori(0, LAST) as b:
                body(b, False)
                seam(b + 1, True)
            body(LAST, True)
            for r in range(RT):
                add_bias(LAST, 1, r)
            for r in range(RT):
                row_stats(LAST, 1, r)
                stats_written(LAST, r)
                row_aggregate(LAST, r)
            for r in range(RT):
                row_normalise(LAST, r)

        @block.gpsimd
        def _(pool):
            nc.gpsimd.memset(ones[:, :], 1.0).then_inc(pool_const, 1)
            nc.gpsimd.memset(exps[:, :], -0.5).then_inc(pool_chain, 1)
            nc.gpsimd.memset(ln_eps[:, :], LN_EPS).then_inc(pool_chain, 1)
            pool.wait_ge(pool_chain, POOL_CONSTS)
            pool.wait_ge(var_eps, 1)
            nc.gpsimd.tensor_tensor(scale[:, :], scale[:, :], exps[:, :], ALU.pow).then_inc(rstd_bn, 1)
            pool.wait_ge(var_eps, 2)
            pool.dma_start(bias_part[0:1, :], rows[2:3, :]).then_inc(outb_loaded, 16)
            for j in range(FOLD):
                f, k = divmod(j, K)
                for n in range(H):
                    pool.wait_ge(bank_free, H * j + n + 1)
                    pool.dma_start(folded[f, n, k // 2, :, k % 2, :],
                                   fold_out[:, n * N:(n + 1) * N]).then_inc(fold_stored[n], 16)
            for n in range(H):
                pool.wait_ge(fold_stored[n], 16 * FOLD)
            pool.wait_ge(bias_done, 1)
            pool.dma_start(ln_gamma[:, :], rows[0:1, :].to_broadcast([P, D])).then_inc(ln_loaded, 16)
            pool.dma_start(ln_beta[:, :], rows[1:2, :].to_broadcast([P, D])).then_inc(ln_loaded, 16)
            pool.wait_ge(ln_loaded, 32)

            STAGES = 2

            def inverse_deviation(b, r):
                done = STAGES * RT * b + (POOL_CONSTS + r)
                pool.wait_ge(mv_ready, RT * b + (r + 1))
                nc.gpsimd.tensor_tensor(rstd[:, r:r + 1], mv[:, r, 1:2], ln_eps[:, :], ALU.add).then_inc(pool_chain, 1)
                pool.wait_ge(pool_chain, done + 1)
                nc.gpsimd.tensor_tensor(rstd[:, r:r + 1], rstd[:, r:r + 1], exps[:, 0:1],
                                        ALU.pow).then_inc(rstd_ready, 1)

            def finish_rows(b, r):
                row = y[:, r, :]
                done = STAGES * RT * b + (POOL_CONSTS + RT + r)
                pool.wait_ge(y_normal, RT * b + (r + 1))
                nc.gpsimd.tensor_tensor(row, row, ln_gamma[:, :], ALU.mult).then_inc(pool_chain, 1)
                pool.wait_ge(pool_chain, done + 1)
                nc.gpsimd.tensor_tensor(row, row, ln_beta[:, :], ALU.add).then_inc(y_final, 1)

            with pool.Fori(0, BLOCKS) as b:
                for r in range(RT):
                    inverse_deviation(b, r)
                for r in range(RT):
                    finish_rows(b, r)


def kernel(**inputs):
    import numpy as np
    import concourse.bacc as bacc
    from concourse.bass_utils import run_bass_kernel_spmd

    g = {k.replace("L0_rec_", ""): np.asarray(v) for k, v in inputs.items()}

    def columns(v):
        return v.reshape(-1, P).T

    def lhs_chunks(w):
        return w.reshape(K, P, K, P).transpose(2, 1, 0, 3).reshape(K, P, D)

    out_w = g["out_w"]
    arrays = {
        "x_blocks": g["r_x"].reshape(BLOCKS, R, K, P).transpose(0, 3, 2, 1),
        "stream": np.concatenate([lhs_chunks(g["linear_w"].T), lhs_chunks(g["proj_w"].T),
                                  lhs_chunks(g["deep1_w"]), lhs_chunks(g["cross_w"].T),
                                  lhs_chunks(g["deep2_w"])]),
        "out_rows": out_w.reshape(OUT_TILES, P, D),
        "out_deep": out_w[D:2 * D].reshape(K // 2, 2, P, H, N).transpose(3, 0, 2, 1, 4)
                    .reshape(H, K // 2, P, 2 * N),
        "params": np.concatenate([columns(g[n]) for n in (
            "bn_gamma", "bn_beta", "bn_mean", "bn_var", "linear_b", "deep1_b", "deep2_b",
            "cross_b", "proj_b")], axis=1),
        "rows": np.stack([g["ln_gamma"], g["ln_beta"], g["out_b"]]),
    }
    arrays = {k: np.ascontiguousarray(v) for k, v in arrays.items()}

    nc = bacc.Bacc("TRN2", target_bir_lowering=False, num_devices=1)
    args = [nc.dram_tensor(k, v.shape, mybir.dt.from_np(v.dtype), kind="ExternalInput").ap()
            for k, v in arrays.items()]
    out = nc.dram_tensor("out", (ROWS, D), F32, kind="ExternalOutput").ap()
    rec_tower(nc, *args, out)
    r = run_bass_kernel_spmd(nc, [arrays], core_ids=[0])
    return r.results[0]["out"]
```

```python
from contextlib import ExitStack

import concourse.bass as bass
from concourse import mybir

P = 128
ROWS, D = 2048, 1024
K = D // P
R = 512
BLOCKS = ROWS // R
RT = R // P
N = 512
H = D // N
RING = 4
SPLIT = 2
TILES = 3 * K
HALF = 3 * K // 2
STEPS = TILES + H * HALF
FOLD = 2 * K
OUT_TILES = 3 * K
BN_EPS, LN_EPS = 1e-3, 1e-6

F32 = mybir.dt.float32
F32R = mybir.dt.float32r
ALU = mybir.AluOpType
ACT = mybir.ActivationFunctionType

GAMMA, BETA, MEAN, VAR = (i * 3 * K for i in range(4))
LIN_B, DEEP1_B, DEEP2_B, CROSS_B, PROJ_B = (12 * K + i * K for i in range(5))
PARAMS = 17 * K

OUT_ORDER = list(range(K)) + [t for k in range(K) for t in (2 * K + k, K + k)]


def rec_tower(nc, x_blocks, stream, out_rows, out_deep, params, rows, out):
    ctx = ExitStack()
    with ctx:
        def sb(name, shape, dt=F32):
            return ctx.enter_context(nc.sbuf_tensor(name, shape, dt))

        def sem(name):
            return ctx.enter_context(nc.semaphore(name))

        folded = nc.dram_tensor("folded", [2, H, K // 2, P, 2, N], F32, kind="Internal").ap()

        XH = sb("XH", [P, 4, K, R], F32R)
        CH = sb("CH", [P, 4, K, R], F32R)
        x_raw = sb("x_raw", [P, K, R])
        w_raw = sb("w_raw", [P, RING, D])
        w_split = sb("w_split", [P, SPLIT, 2, D], F32R)
        y = sb("y", [P, RT, D])
        bias_row = sb("bias_row", [P, D])
        ln_gamma = sb("ln_gamma", [P, D])
        ln_beta = sb("ln_beta", [P, D])
        prm = sb("prm", [P, PARAMS])
        scale = sb("scale", [P, 3 * K])
        shift = sb("shift", [P, 3 * K])
        exps = sb("exps", [P, 3 * K])
        ln_eps = sb("ln_eps", [P, 1])
        ones = sb("ones", [P, P])
        stats = sb("stats", [P, RT, H, 6])
        mv = sb("mv", [P, RT, 2])
        rstd = sb("rstd", [P, RT])
        bank = ctx.enter_context(nc.psum_tensor("bank", [P, 8, N], F32))
        bias_part, fold_out = ln_gamma, ln_beta

        prm_loaded = sem("prm_loaded")
        x_loaded = sem("x_loaded")
        ln_loaded = sem("ln_loaded")
        w_loaded = [sem(f"w_loaded{i}") for i in range(RING)]
        y_moved = [sem(f"y_moved{i}") for i in range(RING)]
        outb_loaded = sem("outb_loaded")
        pool_const = sem("pool_const")
        rstd_bn = sem("rstd_bn")
        var_eps = sem("var_eps")
        vec_chain = sem("vec_chain")
        pool_chain = sem("pool_chain")
        w_scaled = sem("w_scaled")
        w_hi = sem("w_hi")
        w_ready = sem("w_ready")
        out_hi = sem("out_hi")
        out_used = sem("out_used")
        rhs_ready = sem("rhs_ready")
        x_hi = sem("x_hi")
        x_ready = sem("x_ready")
        chunk_done = sem("chunk_done")
        bank_free = sem("bank_free")
        bias_done = sem("bias_done")
        fold_stored = [sem(f"fold_stored{n}") for n in range(H)]
        silu_done = sem("silu_done")
        tile_done = sem("tile_done")
        z_biased = sem("z_biased")
        stats_ready = sem("stats_ready")
        mv_ready = sem("mv_ready")
        rstd_ready = sem("rstd_ready")
        y_centred = sem("y_centred")
        y_final = sem("y_final")
        tail_rows = sem("tail_rows")
        y_scaled = sem("y_scaled")
        tail_pool = sem("tail_pool")
        tail_final = sem("tail_final")

        LAST = BLOCKS - 1
        POOL_CONSTS = 2
        WARM = 26
        WIDE = 4
        EARLY = 6
        FOLD_RESULTS = [[]] * 3 + [[0, 1, 2], [3, 4]] + [[t] for t in range(5, FOLD)]
        FOLD_TILES = [[6, 7], [8, 9], [10, 11], [12, 13], [14, 15], [16, 17], [18, 19, 20], [21, 22, 23]] + [[]] * K
        BANKS_FOLD = H * FOLD + H
        Y_FOLD = 16 * (OUT_TILES // RING)

        block = ctx.enter_context(nc.Block())

        @block.sync
        def _(sp):
            def load_chunk(c, slot, src):
                if not isinstance(c, int) or c >= RING:
                    sp.wait_ge(w_ready, c - RING + 1)
                sp.dma_start(w_raw[:, slot, :], src).then_inc(w_loaded[slot], 16)

            def load_out_tile(i):
                if i >= RING:
                    sp.wait_ge(out_used, i - RING + 1)
                sp.dma_start(y[:, i % RING, :], out_rows[OUT_ORDER[i]]).then_inc(y_moved[i % RING], 16)

            def fold_chunk(c):
                if c < FOLD:
                    load_chunk(c, c % RING, stream[c])

            sp.dma_start(prm[:, :], params).then_inc(prm_loaded, 16)
            fold_chunk(0)
            load_out_tile(0)
            load_out_tile(1)
            fold_chunk(1)
            load_out_tile(2)
            load_out_tile(3)
            fold_chunk(2)
            fold_chunk(3)
            for i in range(RING, K):
                load_out_tile(i)
            for j in range(K):
                load_out_tile(K + 2 * j)
                load_out_tile(K + 2 * j + 1)
                fold_chunk(RING + j)
                if j == 2:
                    sp.dma_start(x_raw[:, :, :], x_blocks[0]).then_inc(x_loaded, 16)
            for c in range(RING + K, FOLD):
                fold_chunk(c)

            def first(b):
                return FOLD + STEPS * b

            def tile_loads(b):
                with sp.Fori(0, TILES // RING) as t:
                    for u in range(RING):
                        i = t * RING + u
                        load_chunk(first(b) + i, u, stream[bass.ds(i + FOLD, 1)].rearrange("a p n -> (a p) n"))

            def x_load(b):
                sp.wait_ge(tile_done, TILES * (b - 1) + 2 * K)
                sp.wait_ge(x_ready, K * b)
                sp.dma_start(x_raw[:, :, :],
                             x_blocks[bass.ds(b, 1)].rearrange("a p k r -> (a p) k r")).then_inc(x_loaded, 16)

            def z_loads(b):
                for n in range(H):
                    for q in range(HALF):
                        src = out_deep[n, q - K] if q >= K else folded[q // (K // 2), n, q % (K // 2)].rearrange(
                            "p a n -> p (a n)")
                        load_chunk(first(b) + TILES + HALF * n + q, q % RING, src)

            def stores(b):
                for r in range(RT):
                    sp.wait_ge(y_final, RT * b + (r + 1))
                    sp.dma_start(out[bass.ds((RT * b + r) * P, P), :], y[:, r, :]).then_inc(y_moved[r], 16)

            tile_loads(0)
            for n in range(H):
                sp.wait_ge(fold_stored[n], 16 * FOLD)
            with sp.Fori(0, LAST) as b:
                x_load(b + 1)
                z_loads(b)
                tile_loads(b + 1)
                stores(b)
            z_loads(LAST)
            for r in range(RT):
                for n in range(H):
                    if r < RT - 1:
                        sp.wait_ge(tail_pool, H * r + n + 1)
                    else:
                        sp.wait_ge(tail_final, n + 1)
                    sp.dma_start(out[(RT * LAST + r) * P:(RT * LAST + r + 1) * P, n * N:(n + 1) * N],
                                 y[:, r, n * N:(n + 1) * N]).then_inc(y_moved[r], 16)
            for r in range(RT):
                sp.wait_ge(y_moved[r], Y_FOLD + 16 * (LAST + H))

        @block.tensor
        def _(pe):
            def three(out_ap, hi_l, lo_l, hi_r, lo_r, start, stop):
                nc.tensor.matmul(out_ap, hi_l, hi_r, start=start, stop=False)
                nc.tensor.matmul(out_ap, hi_l, lo_r, start=False, stop=False)
                return nc.tensor.matmul(out_ap, lo_l, hi_r, start=False, stop=stop)

            def half_of_chunk(c, h):
                return w_split[:, c % SPLIT, h, :].rearrange("p (k m) -> p k m", k=K)

            def fold_tile(out_banks, hi, lo, rhs, k, tile=None):
                for n in range(H):
                    if tile is not None:
                        pe.wait_ge(bank_free, H * (tile - 4) + n + 1)
                    nc.tensor.matmul(out_banks[n], hi, rhs[:, n, k, :], start=k == 0, stop=False)
                    nc.tensor.matmul(out_banks[n], hi, rhs[:, 2 + n, k, :], start=False, stop=False)
                for n in range(H):
                    last = nc.tensor.matmul(out_banks[n], lo, rhs[:, n, k, :], start=False, stop=k == K - 1)
                return last

            pe.wait_ge(pool_const, 1)
            for _ in range(WARM):
                nc.tensor.matmul(bank[:, 7, 0:P], ones[:, :], ones[:, :], start=True, stop=True)

            for q in range(WIDE):
                pe.wait_ge(w_ready, q + 1)
                hi, lo = (w_split[:, q % SPLIT, h, :].rearrange("p (a m) -> p a m", a=2) for h in range(2))
                for a in range(2):
                    pe.wait_ge(rhs_ready, 2 * q + a + 1)
                    for m in range(4):
                        last = fold_tile([bank[:, H * m + n, :] for n in range(H)],
                                         hi[:, a, m * P:(m + 1) * P], lo[:, a, m * P:(m + 1) * P],
                                         XH, 2 * q + a)
                last.then_inc(chunk_done, 1)

            def fold_chunks(f, rhs, base):
                for u in range(4):
                    c = base + u
                    hi, lo = half_of_chunk(u, 0), half_of_chunk(u, 1)
                    pe.wait_ge(w_ready, c + 1)
                    for k in range(K):
                        pe.wait_ge(rhs_ready, f * K + k + 1)
                        last = fold_tile([bank[:, H * u + n, :] for n in range(H)],
                                         hi[:, k, :], lo[:, k, :], rhs, k, None if k else c)
                    last.then_inc(chunk_done, 1)

            fold_chunks(0, XH, 4)
            with pe.Fori(0, K // 4) as t:
                fold_chunks(1, CH, t * 4 + K)
            pe.wait_ge(bank_free, H * FOLD - H)
            pe.wait_ge(out_used, OUT_TILES)
            for n in range(H):
                last = nc.tensor.matmul(bank[:, 4 + n, :], ones[:, :], bias_part[:, n * N:(n + 1) * N],
                                        start=True, stop=True)
            last.then_inc(bias_done, 1)

            def feature_tiles(b, at, src):
                for m in range(K):
                    c = FOLD + STEPS * b + at + m
                    hi, lo = half_of_chunk(m, 0), half_of_chunk(m, 1)
                    pe.wait_ge(w_ready, c + 1)
                    if at == 0 and m == 0:
                        pe.wait_ge(bank_free, 2 * RT * b + BANKS_FOLD - RT)
                    elif at == 0 and m == RT:
                        pe.wait_ge(bank_free, 2 * RT * b + BANKS_FOLD)
                    elif at:
                        pe.wait_ge(tile_done, TILES * b + (at + m - K + 1))
                    for k in range(K):
                        if at == 0 and m == 0:
                            pe.wait_ge(x_ready, K * b + k + 1)
                        last = three(bank[:, m, :], hi[:, k, :], lo[:, k, :],
                                     XH[:, src, k, :], XH[:, src + 1, k, :], k == 0, k == K - 1)
                    last.then_inc(chunk_done, 1)

            def z_half(b, n, tail=False):
                for q in range(HALF - SPLIT * tail):
                    c = FOLD + STEPS * b + TILES + HALF * n + q
                    pe.wait_ge(w_ready, c + 1)
                    if q == 0:
                        pe.wait_ge(tile_done, TILES * b + (TILES - K + RT) + RT * n)
                    if q == K:
                        pe.wait_ge(tile_done, TILES * b + TILES)
                    for a in range(2):
                        for r in range(RT):
                            last = z_tile(n, q, a, r)
                    last.then_inc(chunk_done, 1)
                if tail:
                    for r, q in ((0, -2), (1, -2), (0, -1), (1, -1), (2, -2), (2, -1), (3, -2), (3, -1)):
                        q += HALF
                        pe.wait_ge(w_ready, FOLD + STEPS * LAST + TILES + HALF * n + q + 1)
                        for a in range(2):
                            last = z_tile(n, q, a, r)
                        if q == HALF - 1:
                            last.then_inc(tail_rows, 1)

            def z_tile(n, q, a, r):
                act, at = ((XH, 0), (CH, 0), (CH, 2))[q // (K // 2)]
                k = 2 * (q % (K // 2)) + a
                return three(bank[:, bass.ds(RT * n + r, 1), :].rearrange("p a n -> p (a n)"),
                             act[:, at, k, r * P:(r + 1) * P], act[:, at + 1, k, r * P:(r + 1) * P],
                             w_split[:, q % SPLIT, 0, a * N:(a + 1) * N],
                             w_split[:, q % SPLIT, 1, a * N:(a + 1) * N],
                             q == 0 and a == 0, q == HALF - 1 and a == 1)

            def features(b):
                feature_tiles(b, 0, 0)
                feature_tiles(b, K, 0)
                feature_tiles(b, 2 * K, 2)

            features(0)
            with pe.Fori(0, LAST) as b:
                with pe.Fori(0, H) as n:
                    z_half(b, n)
                features(b + 1)
            z_half(LAST, 0)
            z_half(LAST, 1, tail=True)

        @block.scalar
        def _(act):
            def split_hi(c, slot):
                if isinstance(c, int) and c < FOLD:
                    act.wait_ge(w_scaled, c + 1)
                else:
                    act.wait_ge(w_loaded[slot], 4 * (c - slot) + 16)
                if not isinstance(c, int) or c >= SPLIT:
                    act.wait_ge(chunk_done, c - SPLIT + 1)
                nc.scalar.activation(w_split[:, slot % SPLIT, 0, :], w_raw[:, slot, :], ACT.Copy).then_inc(w_hi, 1)

            def out_tile_hi(i):
                if i >= K and (i - K) % 2:
                    return
                act.wait_ge(y_moved[i % RING], 16 * (i // RING + 1))
                dst, k = (XH, i) if i < K else (CH, (i - K) // 2)
                nc.scalar.activation(dst[:, 0:H, k, :], y[:, i % RING, :].rearrange("p (h n) -> p h n", h=H),
                                     ACT.Copy).then_inc(out_hi, 1)

            def x_split_hi(b, k):
                act.wait_ge(x_loaded, 16 * b + 16)
                nc.scalar.activation(XH[:, 0, k, :], x_raw[:, k, :], ACT.Copy).then_inc(x_hi, 1)

            def silu_tile(c, bank_at, bias_at, done):
                act.wait_ge(chunk_done, c + 1)
                nc.scalar.activation(bank_at, bank_at, ACT.Silu, bias=bias_at).then_inc(done, 1)

            def fold_result(t):
                act.wait_ge(chunk_done, max(t, WIDE - 1) + 1)
                for n in range(H):
                    if t:
                        act.wait_ge(fold_stored[n], 16 * t)
                    nc.scalar.activation(fold_out[:, n * N:(n + 1) * N], bank[:, H * (t % 4) + n, :],
                                         ACT.Copy).then_inc(bank_free, 1)

            act.wait_ge(var_eps, 2)
            act.dma_start(bias_part[0:1, :], rows[2:3, :]).then_inc(outb_loaded, 16)

            split_hi(0, 0)
            out_tile_hi(0)
            out_tile_hi(1)
            split_hi(1, 1)
            for i in range(2, EARLY):
                out_tile_hi(i)
            for j in range(FOLD):
                for t in FOLD_RESULTS[j][:1]:
                    fold_result(t)
                split_hi(j + SPLIT, (j + SPLIT) % RING)
                for t in FOLD_RESULTS[j][1:]:
                    fold_result(t)
                for i in FOLD_TILES[j]:
                    out_tile_hi(i)
                if K - 1 <= j < 2 * K - 1:
                    x_split_hi(0, j - (K - 1))
            act.wait_ge(bias_done, 1)
            for n in range(H):
                nc.scalar.activation(bias_row[:, n * N:(n + 1) * N], bank[:, 4 + n, :], ACT.Copy).then_inc(bank_free, 1)

            def silu_z(b, n, r):
                act.wait_ge(y_moved[r], 16 * b + Y_FOLD)
                act.wait_ge(z_biased, 2 * RT * b + RT * n + r + 1)
                nc.scalar.activation(y[:, r, n * N:(n + 1) * N], bank[:, RT * n + r, :],
                                     ACT.Silu).then_inc(bank_free, 1)

            def first(b):
                return FOLD + STEPS * b

            def h_tile(b, j, m, slot, bias_at):
                c = first(b) + j
                split_hi(c + SPLIT, (slot + SPLIT) % RING)
                silu_tile(c, bank[:, bass.ds(m, 1), :].rearrange("p a n -> p (a n)"),
                          prm[:, bass.ds(bias_at + m, 1)], silu_done)

            def seam(b, z):
                for j in range(K):
                    h_tile(b, j, j, j % RING, DEEP1_B)
                    if z and j < 2:
                        for r in (2 * j, 2 * j + 1):
                            silu_z(b - 1, 1, r)

            def body(b, last):
                with act.Fori(0, K // RING) as t:
                    for u in range(RING):
                        split_hi(first(b) + t * RING + (K + u + SPLIT), (u + SPLIT) % RING)
                with act.Fori(0, K // RING) as t:
                    for u in range(RING):
                        m = t * RING + u
                        h_tile(b, m + 2 * K, m, u, DEEP2_B)
                with act.Fori(0, HALF // RING) as t:
                    for u in range(RING):
                        split_hi(first(b) + t * RING + (TILES + u + SPLIT), (u + SPLIT) % RING)
                for q in range(HALF):
                    j = TILES + HALF + q
                    if not (last and q >= HALF - SPLIT):
                        split_hi(first(b) + j + SPLIT, (j + SPLIT) % RING)
                    if q < 2:
                        for r in (2 * q, 2 * q + 1):
                            silu_z(b, 0, r)
                    if not last and K // 2 - 1 <= q < K // 2 - 1 + K:
                        x_split_hi(b + 1, q - (K // 2 - 1))

            seam(0, False)
            with act.Fori(0, LAST) as b:
                body(b, False)
                seam(b + 1, True)
            body(LAST, True)

            def scale_rows(r):
                act.wait_ge(y_centred, RT * LAST + r + 1)
                act.wait_ge(rstd_ready, RT * LAST + r + 1)
                nc.scalar.activation(y[:, r, :], y[:, r, :], ACT.Copy, scale=rstd[:, r:r + 1]).then_inc(y_scaled, 1)

            silu_z(LAST, 1, 0)
            for r in range(1, RT):
                silu_z(LAST, 1, r)
                scale_rows(r - 1)

        @block.vector
        def _(dve):
            chain = [0]

            def link(ins):
                chain[0] += 1
                ins.then_inc(vec_chain, 1)
                dve.wait_ge(vec_chain, chain[0])

            dve.wait_ge(prm_loaded, 16)
            nc.vector.tensor_scalar(scale[:, :], prm[:, VAR:VAR + 3 * K], BN_EPS, None, ALU.add).then_inc(var_eps, 1)
            nc.vector.memset(bias_part[:, :], 0.0).then_inc(var_eps, 1)
            dve.wait_ge(rstd_bn, 1)
            link(nc.vector.tensor_tensor(scale[:, 0:K], scale[:, 0:K], prm[:, GAMMA:GAMMA + K], ALU.mult))

            def bn_shift():
                dve.wait_ge(rstd_bn, 2)
                link(nc.vector.tensor_tensor(scale[:, K:3 * K], scale[:, K:3 * K],
                                             prm[:, GAMMA + K:GAMMA + 3 * K], ALU.mult))
                link(nc.vector.tensor_scalar(shift[:, :], prm[:, MEAN:MEAN + 3 * K], -1.0, None, ALU.mult))
                link(nc.vector.tensor_tensor(shift[:, 0:K], shift[:, 0:K], prm[:, LIN_B:LIN_B + K], ALU.add))
                link(nc.vector.tensor_tensor(shift[:, 2 * K:3 * K], shift[:, 2 * K:3 * K],
                                             prm[:, PROJ_B:PROJ_B + K], ALU.add))
                link(nc.vector.tensor_tensor(shift[:, :], shift[:, :], scale[:, :], ALU.mult))
                link(nc.vector.tensor_tensor(shift[:, :], shift[:, :], prm[:, BETA:BETA + 3 * K], ALU.add))

            def scale_chunk(c):
                if c >= FOLD:
                    return
                branch = 0 if c < K else 2 * K
                dve.wait_ge(w_loaded[c % RING], 16 * (c // RING + 1))
                at, k = (2 * c, 2) if c < WIDE else (branch, K)
                ap = w_raw[:, c % RING, :].rearrange("p (k m) -> p k m", k=k)
                nc.vector.tensor_tensor(ap, ap, scale[:, at:at + k].unsqueeze(2).to_broadcast([P, k, D // k]),
                                        ALU.mult).then_inc(w_scaled, 1)

            def split_lo(c, slot):
                dve.wait_ge(w_hi, c + 1)
                nc.vector.tensor_tensor(w_split[:, slot % SPLIT, 1, :], w_raw[:, slot, :],
                                        w_split[:, slot % SPLIT, 0, :].bitcast(F32),
                                        ALU.subtract).then_inc(w_ready, 1)

            def out_tile_lo(i):
                src = y[:, i % RING, :]
                if i < K or (i - K) % 2 == 0:
                    dst, k = (XH, i) if i < K else (CH, (i - K) // 2)
                    dve.wait_ge(out_hi, (i if i < K else K + (i - K) // 2) + 1)
                    nc.vector.tensor_tensor(dst[:, 2:4, k, :], src.rearrange("p (h n) -> p h n", h=H),
                                            dst[:, 0:2, k, :].bitcast(F32), ALU.subtract).then_inc(rhs_ready, 1)
                else:
                    dve.wait_ge(y_moved[i % RING], 16 * (i // RING + 1))

            def out_tile_sum(i):
                src = y[:, i % RING, :]
                t = OUT_ORDER[i]
                if i == 0:
                    dve.wait_ge(outb_loaded, 16)
                else:
                    dve.wait_ge(out_used, i)
                nc.vector.scalar_tensor_tensor(out=bias_part[:, :], in0=src, scalar=shift[:, t:t + 1],
                                               in1=bias_part[:, :], op0=ALU.mult, op1=ALU.add).then_inc(out_used, 1)

            def out_tile(i):
                out_tile_lo(i)
                out_tile_sum(i)

            def x_split_lo(b, k):
                dve.wait_ge(x_hi, K * b + k + 1)
                nc.vector.tensor_tensor(XH[:, 1, k, :], x_raw[:, k, :], XH[:, 0, k, :].bitcast(F32),
                                        ALU.subtract).then_inc(x_ready, 1)

            scale_chunk(0)
            split_lo(0, 0)
            out_tile_lo(0)
            out_tile_lo(1)
            bn_shift()
            out_tile_sum(0)
            scale_chunk(1)
            split_lo(1, 1)
            out_tile_sum(1)
            for i in range(2, EARLY):
                out_tile(i)
                if i == 2:
                    scale_chunk(SPLIT)
            for j in range(FOLD):
                split_lo(j + SPLIT, (j + SPLIT) % RING)
                scale_chunk(j + SPLIT + 1)
                for i in FOLD_TILES[j]:
                    out_tile(i)
                if K - 1 <= j < 2 * K - 1:
                    x_split_lo(0, j - (K - 1))
            dve.wait_ge(bank_free, BANKS_FOLD)

            def first(b):
                return FOLD + STEPS * b

            def at(tensor, m):
                return tensor[:, bass.ds(m, 1), :].rearrange("p a n -> p (a n)")

            def h1_tile(b, j, slot):
                split_lo(first(b) + j + SPLIT, (slot + SPLIT) % RING)
                dve.wait_ge(silu_done, 2 * K * b + (j + 1))
                nc.vector.tensor_copy(XH[:, 2, j, :], bank[:, j, :]).then_inc(vec_chain, 1)
                dve.wait_ge(vec_chain, chain_at(b, H1_LINK + j))
                nc.vector.tensor_tensor(XH[:, 3, j, :], bank[:, j, :], XH[:, 2, j, :].bitcast(F32),
                                        ALU.subtract).then_inc(tile_done, 1)

            H1_LINK, C_LINK, H2_LINK, LINKS = 1, K + 1, 3 * K + 1, 4 * K
            chain_before = chain[0]

            def chain_at(b, i):
                return LINKS * b + (chain_before + i)

            def c_tile(b, m, slot):
                split_lo(first(b) + K + m + SPLIT, (slot + SPLIT) % RING)
                dve.wait_ge(chunk_done, first(b) + K + m + 1)
                acc = at(bank, m)
                bias = prm[:, bass.ds(CROSS_B + m, 1)]
                nc.vector.tensor_tensor(acc, acc, at(x_raw, m), ALU.mult).then_inc(vec_chain, 1)
                dve.wait_ge(vec_chain, chain_at(b, 2 * m + C_LINK))
                nc.vector.tensor_scalar(at(CH[:, 0], m), acc, bias, None, ALU.add).then_inc(vec_chain, 1)
                dve.wait_ge(vec_chain, chain_at(b, 2 * m + C_LINK + 1))
                nc.vector.scalar_tensor_tensor(out=at(CH[:, 1], m), in0=acc, scalar=bias,
                                               in1=at(CH[:, 0], m).bitcast(F32), op0=ALU.add,
                                               op1=ALU.subtract).then_inc(tile_done, 1)

            def h2_tile(b, m, slot):
                split_lo(first(b) + 2 * K + m + SPLIT, (slot + SPLIT) % RING)
                dve.wait_ge(silu_done, 2 * K * b + K + m + 1)
                acc = at(bank, m)
                s = scale[:, bass.ds(K + m, 1)]
                nc.vector.tensor_scalar(at(CH[:, 2], m), acc, s, None, ALU.mult).then_inc(vec_chain, 1)
                dve.wait_ge(vec_chain, chain_at(b, m + H2_LINK))
                nc.vector.scalar_tensor_tensor(out=at(CH[:, 3], m), in0=acc, scalar=s,
                                               in1=at(CH[:, 2], m).bitcast(F32), op0=ALU.mult,
                                               op1=ALU.subtract).then_inc(tile_done, 1)

            def add_bias(b, n, r):
                if isinstance(b, int) and b == LAST and n:
                    dve.wait_ge(tail_rows, r + 1)
                else:
                    dve.wait_ge(chunk_done, first(b) + TILES + HALF * (n + 1))
                nc.vector.tensor_tensor(bank[:, RT * n + r, :], bank[:, RT * n + r, :],
                                        bias_row[:, n * N:(n + 1) * N], ALU.add).then_inc(z_biased, 1)

            def row_stats(b, n, r):
                dve.wait_ge(bank_free, 2 * RT * b + (BANKS_FOLD + RT * n + r + 1))
                nc.vector.bn_stats(stats[:, r, n, :], y[:, r, n * N:(n + 1) * N]).then_inc(stats_ready, 1)

            def stats_written(b, r):
                dve.wait_ge(stats_ready, 2 * RT * b + (RT + r + 1))

            def row_aggregate(b, r):
                nc.vector.bn_aggr(mv[:, r, :], stats[:, r, :, :].rearrange("p h s -> p (h s)")).then_inc(mv_ready, 1)

            def row_centre(b, r):
                dve.wait_ge(ln_loaded, 32)
                dve.wait_ge(mv_ready, RT * b + (r + 1))
                nc.vector.scalar_tensor_tensor(out=y[:, r, :], in0=y[:, r, :], scalar=mv[:, r, 0:1],
                                               in1=ln_gamma[:, :], op0=ALU.subtract,
                                               op1=ALU.mult).then_inc(y_centred, 1)

            def row_finish(b, r, lo, hi, done):
                dve.wait_ge(y_centred, RT * b + (r + 1))
                dve.wait_ge(rstd_ready, RT * b + (r + 1))
                nc.vector.scalar_tensor_tensor(out=y[:, r, lo:hi], in0=y[:, r, lo:hi], scalar=rstd[:, r:r + 1],
                                               in1=ln_beta[:, lo:hi], op0=ALU.mult, op1=ALU.add).then_inc(done, 1)

            def seam(b, z):
                for j in range(K):
                    if z and 2 <= j < 2 + RT:
                        stats_written(b - 1, j - 2)
                    h1_tile(b, j, j % RING)
                    if z and j < 2:
                        for r in (2 * j, 2 * j + 1):
                            add_bias(b - 1, 1, r)
                    if z and 1 <= j < 3:
                        for r in (2 * j - 2, 2 * j - 1):
                            row_stats(b - 1, 1, r)
                    if z and 3 <= j < 3 + RT:
                        row_finish(b - 1, j - 3, 0, D, y_final)
                    if z and 2 <= j < 2 + RT:
                        row_aggregate(b - 1, j - 2)
                        row_centre(b - 1, j - 2)

            def body(b, last):
                with dve.Fori(0, K // RING) as t:
                    for u in range(RING):
                        c_tile(b, t * RING + u, u)
                with dve.Fori(0, K // RING) as t:
                    for u in range(RING):
                        h2_tile(b, t * RING + u, u)
                with dve.Fori(0, HALF // RING) as t:
                    for u in range(RING):
                        split_lo(first(b) + t * RING + (TILES + u + SPLIT), (u + SPLIT) % RING)
                for q in range(HALF):
                    if not (last and q >= HALF - SPLIT):
                        split_lo(first(b) + TILES + HALF + q + SPLIT, (q + SPLIT) % RING)
                    if q < 2:
                        for r in (2 * q, 2 * q + 1):
                            add_bias(b, 0, r)
                    if 1 <= q < 3:
                        for r in (2 * q - 2, 2 * q - 1):
                            row_stats(b, 0, r)
                    if not last and K // 2 - 1 <= q < K // 2 - 1 + K:
                        x_split_lo(b + 1, q - (K // 2 - 1))

            seam(0, False)
            with dve.Fori(0, LAST) as b:
                body(b, False)
                seam(b + 1, True)
            body(LAST, True)

            def tail_stats(r):
                row_stats(LAST, 1, r)
                stats_written(LAST, r)
                row_aggregate(LAST, r)

            add_bias(LAST, 1, 0)
            add_bias(LAST, 1, 1)
            tail_stats(0)
            row_centre(LAST, 0)
            for r in range(1, RT):
                tail_stats(r)
                if r + 1 < RT:
                    add_bias(LAST, 1, r + 1)
                row_centre(LAST, r)
            for n in range(H):
                row_finish(LAST, RT - 1, n * N, (n + 1) * N, tail_final)

        @block.gpsimd
        def _(pool):
            nc.gpsimd.memset(ones[:, :], 1.0).then_inc(pool_const, 1)
            nc.gpsimd.memset(exps[:, :], -0.5).then_inc(pool_chain, 1)
            nc.gpsimd.memset(ln_eps[:, :], LN_EPS).then_inc(pool_chain, 1)
            pool.wait_ge(pool_chain, POOL_CONSTS)
            pool.wait_ge(var_eps, 1)
            for at, n in ((0, K), (K, 2 * K)):
                nc.gpsimd.tensor_tensor(scale[:, at:at + n], scale[:, at:at + n], exps[:, at:at + n],
                                        ALU.pow).then_inc(rstd_bn, 1)
            for j in range(FOLD):
                f, k = divmod(j, K)
                for n in range(H):
                    pool.wait_ge(bank_free, H * j + n + 1)
                    pool.dma_start(folded[f, n, k // 2, :, k % 2, :],
                                   fold_out[:, n * N:(n + 1) * N]).then_inc(fold_stored[n], 16)
            for n in range(H):
                pool.wait_ge(fold_stored[n], 16 * FOLD)
            pool.wait_ge(bias_done, 1)
            pool.dma_start(ln_gamma[:, :], rows[0:1, :].to_broadcast([P, D])).then_inc(ln_loaded, 16)
            pool.dma_start(ln_beta[:, :], rows[1:2, :].to_broadcast([P, D])).then_inc(ln_loaded, 16)
            pool.wait_ge(ln_loaded, 32)

            def inverse_deviation(b, r):
                pool.wait_ge(mv_ready, RT * b + (r + 1))
                nc.gpsimd.tensor_tensor(rstd[:, r:r + 1], mv[:, r, 1:2], ln_eps[:, :], ALU.add).then_inc(pool_chain, 1)
                pool.wait_ge(pool_chain, RT * b + (POOL_CONSTS + r + 1))
                nc.gpsimd.tensor_tensor(rstd[:, r:r + 1], rstd[:, r:r + 1], exps[:, 0:1],
                                        ALU.pow).then_inc(rstd_ready, 1)

            def finish(r):
                pool.wait_ge(y_scaled, r + 1)
                for n in range(H):
                    part = y[:, r, n * N:(n + 1) * N]
                    nc.gpsimd.tensor_tensor(part, part, ln_beta[:, n * N:(n + 1) * N], ALU.add).then_inc(tail_pool, 1)

            with pool.Fori(0, LAST) as b:
                for r in range(RT):
                    inverse_deviation(b, r)
            for r in range(RT):
                inverse_deviation(LAST, r)
                if r:
                    finish(r - 1)


def kernel(**inputs):
    import numpy as np
    import concourse.bacc as bacc
    from concourse.bass_utils import run_bass_kernel_spmd

    g = {k.replace("L0_rec_", ""): np.asarray(v) for k, v in inputs.items()}

    def columns(v):
        return v.reshape(-1, P).T

    def lhs_chunks(w):
        return w.reshape(K, P, K, P).transpose(2, 1, 0, 3).reshape(K, P, D)

    def wide_chunks(w):
        return w[:, :D // 2].reshape(K // 2, 2, P, D // 2).transpose(0, 2, 1, 3).reshape(K // 2, P, D)

    out_w = g["out_w"]
    arrays = {
        "x_blocks": g["r_x"].reshape(BLOCKS, R, K, P).transpose(0, 3, 2, 1),
        "stream": np.concatenate([wide_chunks(g["linear_w"].T), lhs_chunks(g["linear_w"].T)[K // 2:], lhs_chunks(g["proj_w"].T),
                                  lhs_chunks(g["deep1_w"]), lhs_chunks(g["cross_w"].T),
                                  lhs_chunks(g["deep2_w"])]),
        "out_rows": out_w.reshape(OUT_TILES, P, D),
        "out_deep": out_w[D:2 * D].reshape(K // 2, 2, P, H, N).transpose(3, 0, 2, 1, 4)
                    .reshape(H, K // 2, P, 2 * N),
        "params": np.concatenate([columns(g[n]) for n in (
            "bn_gamma", "bn_beta", "bn_mean", "bn_var", "linear_b", "deep1_b", "deep2_b",
            "cross_b", "proj_b")], axis=1),
        "rows": np.stack([g["ln_gamma"], g["ln_beta"], g["out_b"]]),
    }
    arrays = {k: np.ascontiguousarray(v) for k, v in arrays.items()}

    nc = bacc.Bacc("TRN2", target_bir_lowering=False, num_devices=1)
    args = [nc.dram_tensor(k, v.shape, mybir.dt.from_np(v.dtype), kind="ExternalInput").ap()
            for k, v in arrays.items()]
    out = nc.dram_tensor("out", (ROWS, D), F32, kind="ExternalOutput").ap()
    rec_tower(nc, *args, out)
    r = run_bass_kernel_spmd(nc, [arrays], core_ids=[0])
    return r.results[0]["out"]
```
